# Optimizing a Trainium2 kernel written in Bass

```python
import numpy as np
import jax
import jax.numpy as jnp

def _softmax(x, axis=-1):
    return jax.nn.softmax(x, axis=axis)

def _gelu(x):
    return jax.nn.gelu(x, approximate=True)

def _silu(x):
    return jax.nn.silu(x)

def _sigmoid(x):
    return jax.nn.sigmoid(x)

def _layernorm(x, axis=-1, eps=1e-05):
    m = jnp.mean(x, axis=axis, keepdims=True)
    v = jnp.var(x, axis=axis, keepdims=True)
    return (x - m) / jnp.sqrt(v + eps)

def _scatter_add(tgt, idx, src, axis=0):
    return tgt.at[idx].add(src)

def _segment_sum(src, seg, n):
    return jax.ops.segment_sum(src, seg, n)
kernel_name = 'mk_seq_postln_d1_jaxref_r4_a0e41a'

def setup_inputs(seed: int=0):
    np.random.seed(seed)
    _w = jnp.asarray

    def _L0_attn_setup():
        import jax, jax.numpy as jnp
        import numpy as np
        D_MODEL, D_STATE, D_CONV, EXPAND = (256, 16, 4, 2)
        D_INNER = EXPAND * D_MODEL
        BATCH, SEQ = (2, 1024)
        key = jax.random.key(seed)
        ks = jax.random.split(key, 6)
        s = 0.02
        return {'input_tensor': jax.random.normal(ks[0], (BATCH, SEQ, D_MODEL), jnp.float32), 'W_in': jax.random.normal(ks[1], (D_MODEL, 2 * D_INNER), jnp.float32) * s, 'conv_w': jax.random.normal(ks[2], (D_INNER, 1, D_CONV), jnp.float32) * s, 'conv_b': jnp.zeros((D_INNER,), jnp.float32), 'W_x': jax.random.normal(ks[3], (D_INNER, 2 * D_STATE + 1), jnp.float32) * s, 'A_log': jnp.log(jnp.arange(1, D_STATE + 1, dtype=jnp.float32)), 'D_param': jnp.ones((D_INNER,), jnp.float32), 'W_out': jax.random.normal(ks[4], (D_INNER, D_MODEL), jnp.float32) * s}
    _L0_attn_in = _L0_attn_setup()

    def _L0_ffn_setup():
        import jax, jax.numpy as jnp
        import numpy as np
        D_MODEL, D_FF, N_EXP = (256, 1024, 8)
        key = jax.random.key(seed)
        ks = jax.random.split(key, 8)
        s = lambda fan_in: 1.0 / np.sqrt(fan_in)
        x = jax.random.normal(ks[0], (4, 512, D_MODEL), dtype=jnp.float32)
        Wr = jax.random.uniform(ks[1], (N_EXP, D_MODEL), jnp.float32, -s(D_MODEL), s(D_MODEL))
        br = jax.random.uniform(ks[2], (N_EXP,), jnp.float32, -s(D_MODEL), s(D_MODEL))
        W1 = jax.random.uniform(ks[3], (N_EXP, D_FF, D_MODEL), jnp.float32, -s(D_MODEL), s(D_MODEL))
        b1 = jax.random.uniform(ks[4], (N_EXP, D_FF), jnp.float32, -s(D_MODEL), s(D_MODEL))
        W2 = jax.random.uniform(ks[5], (N_EXP, D_MODEL, D_FF), jnp.float32, -s(D_FF), s(D_FF))
        b2 = jax.random.uniform(ks[6], (N_EXP, D_MODEL), jnp.float32, -s(D_FF), s(D_FF))
        return {'x': x, 'Wr': Wr, 'br': br, 'W1': W1, 'b1': b1, 'W2': W2, 'b2': b2}
    _L0_ffn_in = _L0_ffn_setup()
    _d = {'L0_attn_input_tensor': _L0_attn_in['input_tensor'], 'L0_attn_W_in': _L0_attn_in['W_in'], 'L0_attn_conv_w': _L0_attn_in['conv_w'], 'L0_attn_conv_b': _L0_attn_in['conv_b'], 'L0_attn_W_x': _L0_attn_in['W_x'], 'L0_attn_A_log': _L0_attn_in['A_log'], 'L0_attn_D_param': _L0_attn_in['D_param'], 'L0_attn_W_out': _L0_attn_in['W_out'], 'L0_ffn_Wr': _L0_ffn_in['Wr'], 'L0_ffn_br': _L0_ffn_in['br'], 'L0_ffn_W1': _L0_ffn_in['W1'], 'L0_ffn_b1': _L0_ffn_in['b1'], 'L0_ffn_W2': _L0_ffn_in['W2'], 'L0_ffn_b2': _L0_ffn_in['b2']}
    _x0 = _d['L0_attn_input_tensor']
    _d['L0_attn_input_tensor'] = jax.random.normal(jax.random.fold_in(jax.random.key(seed), 1), (1, 4096, 256), dtype=_x0.dtype)
    del _x0
    return _d

def reference(L0_attn_input_tensor, L0_attn_W_in, L0_attn_conv_w, L0_attn_conv_b, L0_attn_W_x, L0_attn_A_log, L0_attn_D_param, L0_attn_W_out, L0_ffn_Wr, L0_ffn_br, L0_ffn_W1, L0_ffn_b1, L0_ffn_W2, L0_ffn_b2):

    def _L0_attn_ref(input_tensor, W_in, conv_w, conv_b, W_x, A_log, D_param, W_out):
        import jax, jax.numpy as jnp
        import numpy as np
        D_MODEL, D_STATE, D_CONV, EXPAND = (256, 16, 4, 2)
        D_INNER = EXPAND * D_MODEL
        BATCH, SEQ = (2, 1024)
        b, seq, _ = input_tensor.shape
        n = D_STATE
        xz = input_tensor @ W_in
        conv_in, gated = (xz[..., :D_INNER], xz[..., D_INNER:])
        y = jax.lax.conv_general_dilated(conv_in.transpose(0, 2, 1), conv_w, window_strides=(1,), padding=[(D_CONV - 1, 0)], dimension_numbers=('NCH', 'OIH', 'NCH'), feature_group_count=D_INNER) + conv_b[None, :, None]
        convolved = jax.nn.silu(y.transpose(0, 2, 1))
        x_dbl = convolved @ W_x
        delta = jax.nn.softplus(x_dbl[..., :1])
        Bm = x_dbl[..., 1:1 + n]
        Cm = x_dbl[..., 1 + n:]
        A = -jnp.exp(A_log)
        deltaA = jnp.exp(delta * A)
        deltaBx = delta * Bm * convolved[..., :n]

        def step(h, inp):
            dA, dBx, c = inp
            h = dA * h + dBx
            return (h, jnp.sum(h * c, axis=-1))
        h0 = jnp.zeros((b, n), convolved.dtype)
        _, ys = jax.lax.scan(step, h0, (deltaA.transpose(1, 0, 2), deltaBx.transpose(1, 0, 2), Cm.transpose(1, 0, 2)))
        ssm_out = ys.T[:, :, None]
        skip_out = ssm_out + convolved * D_param
        gated_out = skip_out * jax.nn.silu(gated)
        return gated_out @ W_out

    def _L0_ffn_ref(x, Wr, br, W1, b1, W2, b2):
        import jax, jax.numpy as jnp
        import numpy as np
        D_MODEL, D_FF, N_EXP = (256, 1024, 8)
        B, S, D = x.shape
        xf = x.reshape(-1, D)
        logits = xf @ Wr.T + br
        expert_idx = jnp.argmax(logits, axis=-1)
        h = jax.nn.relu(jnp.einsum('td,efd->etf', xf, W1) + b1[:, None, :])
        y = jnp.einsum('etf,edf->etd', h, W2) + b2[:, None, :]
        out = y[expert_idx, jnp.arange(xf.shape[0])]
        return out.reshape(B, S, D)
    x = L0_attn_input_tensor
    x = _layernorm(x + _L0_attn_ref(x, L0_attn_W_in, L0_attn_conv_w, L0_attn_conv_b, L0_attn_W_x, L0_attn_A_log, L0_attn_D_param, L0_attn_W_out), axis=-1)
    x = _layernorm(x + _L0_ffn_ref(x, L0_ffn_Wr, L0_ffn_br, L0_ffn_W1, L0_ffn_b1, L0_ffn_W2, L0_ffn_b2), axis=-1)
    return x

_drawn_inputs = setup_inputs


def setup_inputs(seed=0):
    import zlib

    import numpy as np

    out = dict(_drawn_inputs(seed))
    spreads = {'L0_attn_conv_b': (0.0, 0.354), 'L0_attn_D_param': (1.0, 0.6)}
    factors = {'L0_attn_W_in': 3.15,
     'L0_attn_conv_w': 8.0,
     'L0_attn_W_x': 8.0,
     'L0_attn_A_log': 8.0,
     'L0_attn_W_out': 2.937,
     'L0_ffn_b1': 4.035,
     'L0_ffn_b2': 3.17}
    for name, (base, spread) in spreads.items():
        noise = np.random.default_rng([zlib.crc32(name.encode()), seed]).standard_normal(out[name].shape)
        drawn = base * np.exp(spread * noise) if base else spread * noise
        out[name] = jnp.asarray(drawn.astype(out[name].dtype))
    for name, factor in factors.items():
        out[name] = (out[name] * factor).astype(out[name].dtype)
    return out
```

```python
from contextlib import ExitStack

import concourse.bass as bass
from concourse import mybir

ALU = mybir.AluOpType
ACT = mybir.ActivationFunctionType
F32 = mybir.dt.float32
F32R = mybir.dt.float32r
BF16 = mybir.dt.bfloat16
I32 = mybir.dt.int32
AX_X = mybir.AxisListType.X

P = 128
TOKENS = 4096
DM = 256
DI = 512
NST = 16
TAPS = 4
NE = 8
FF = 1024
CH = 512
NCH = TOKENS // CH
SUB = CH // P
KD = DM // P
KI = DI // P
KF = FF // P
B_ROW, C_ROW, XDBL_M = 32, 64, 80
ROW = DM + 1
REGION = TOKENS + P
FILL_ROW0 = NE * REGION
FILL_ID = float(2 * TOKENS)
SLOTS = TOKENS // P - 1 + NE
NTAB = SLOTS + 1
EPS = 1e-5


def build(nc, xT, x, w_in, conv_w, conv_b, w_x, a_log, d_par, w_out, wr, br, w1, b1, w2, b2, out):
    rows = nc.dram_tensor("rows", (FILL_ROW0 + P, ROW), F32, kind="Internal").ap()
    ctx = ExitStack()
    with ctx:
        def sb(name, shape, dt=F32):
            return ctx.enter_context(nc.sbuf_tensor(name, shape, dt))

        def sem(name):
            return ctx.enter_context(nc.semaphore(name))

        ident = sb("ident", [P, P])
        tri = sb("tri", [P, P], BF16)
        ones = sb("ones", [P, P], BF16)
        ones16 = sb("ones16", [NST, P])
        first_w = sb("first_w", [P, NE])
        ebase = sb("ebase", [P, NE])
        slot_no = sb("slot_no", [1, NTAB])
        eps_t = sb("eps_t", [P, 1])
        fill = sb("fill", [P, ROW])
        fill_no = sb("fill_no", [P, 1])
        cw = sb("cw", [P, KI, TAPS])
        cb = sb("cb", [P, KI])
        dp = sb("dp", [P, KI])
        alog = sb("alog", [NST, 1])
        aexp = sb("aexp", [NST, 1])
        aneg = sb("aneg", [NST, 1])
        wr_s = sb("wr_s", [P, KD, NE])
        br_s = sb("br_s", [P, NE])
        win = sb("win", [P, 2, KD, 2 * DI], F32R)
        wraw = sb("wraw", [P, 2 * KD * FF])
        W1N = KD * FF
        WHALF = 2 * W1N
        wsp = sb("wsp", [P, 2, 2 * WHALF], F32R)
        win_raw = wraw[:, 0:KD * 2 * DI]
        wout_raw = wraw[:, KD * 2 * DI:KD * 2 * DI + KI * DM]
        WX0 = KD * 2 * DI + KI * DM
        wx_raw = wraw[:, WX0:WX0 + KI * XDBL_M]
        XS, CS = 2 * 2 * KD * CH, 2 * KI * CH
        xs = wsp[:, 1, 0:XS].rearrange("p (q h k t) -> p q h k t", q=2, h=2, k=KD)
        cvs = wsp[:, 1, XS:XS + CS].rearrange("p (h k t) -> p h k t", h=2, k=KI)
        wout = wsp[:, 0, WHALF:WHALF + 2 * KI * DM].rearrange("p (h k n) -> p h k n", h=2, k=KI)
        WXS = WHALF + 2 * KI * DM
        wx = wsp[:, 0, WXS:WXS + 2 * KI * XDBL_M].rearrange("p (h k n) -> p h k n", h=2, k=KI)
        xraw = sb("xraw", [P, 2, KD, CH])
        xtok = sb("xtok", [P, 2, SUB, DM])
        cin = sb("cin", [P, 2, KI, CH + TAPS - 1])
        acc = sb("acc", [P, KI, CH])
        cv = sb("cv", [P, 2, KI, CH])
        sg = sb("sg", [P, KI, CH])
        gos = sb("gos", [P, 2, KI, CH], F32R)
        x1row = sb("x1row", [P, 2, SUB, ROW])
        x1T = sb("x1T", [P, KD, CH])
        soft = sb("soft", [NST, CH])
        delta = sb("delta", [NST, CH])
        dA = sb("dA", [NST, CH])
        dB = sb("dB", [NST, CH])
        hst = sb("hst", [NST, 2, CH])
        stats = sb("stats", [P, SUB, 6])
        mv = sb("mv", [P, SUB, 2])
        ve = sb("ve", [P, SUB])
        half = sb("half", [P, SUB])
        rstd = sb("rstd", [P, SUB])
        lg = sb("lg", [P, SUB, NE])
        mx = sb("mx", [P, SUB])
        eq = sb("eq", [P, SUB, NE])
        ew = sb("ew", [P, SUB, NE])
        m2 = sb("m2", [P, SUB])
        oh = sb("oh", [P, SUB, NE], BF16)
        p2 = sb("p2", [P, SUB, NE])
        p3 = sb("p3", [P, SUB, NE])
        posf = sb("posf", [P, SUB])
        posi = sb("posi", [P, 2, SUB], I32)
        base = sb("base", [P, 2, NE])
        fillf = sb("fillf", [P, NE])
        filli = sb("filli", [P, NE], I32)
        cnt = sb("cnt", [1, NE])
        cnti = sb("cnti", [1, NE], I32)
        cnts = sb("cnts", [1, NE], I32)
        ntf = sb("ntf", [1, NE])
        nt = sb("nt", [1, NE])
        end = sb("end", [1, NE])
        past = sg[0:1, 0, 0:NTAB * NE].rearrange("p (j e) -> p j e", e=NE)
        pastn = sg[0:1, 1, 0:NTAB * NE].rearrange("p (j e) -> p j e", e=NE)
        ej = sb("ej", [1, NTAB])
        sj = sb("sj", [1, NTAB])
        dj = sb("dj", [1, NTAB])
        rj = sb("rj", [1, NTAB])
        e7 = sb("e7", [1, NTAB])
        fj = sb("fj", [1, NTAB])
        T_ROW, T_E, T_BUF, T_NEXTBUF, T_FIRST = range(5)
        tab = sb("tab", [1, 5, NTAB], I32)
        h = acc[:, 0:2, :]
        hT = gos[:, 0, :, :].rearrange("p k t -> p (k t)").rearrange("p (h b t) -> p h b t", h=2, b=KF)
        xg = gos[:, 1, 0:2, :].rearrange("p k t -> p (k t)").rearrange("p (q h k t) -> p q h k t", q=2, h=2, k=KD)
        cin_flat = cin[:, :, :, :].rearrange("p q k t -> p (q k t)")
        b1b = cin_flat[:, 0:2 * FF].rearrange("p (v f) -> p v f", v=2)
        b2b = cin_flat[:, 2 * FF:2 * FF + 2 * ROW].rearrange("p (v d) -> p v d", v=2)
        xraw_flat = xraw[:, :, :, :].rearrange("p q k t -> p (q k t)")
        xrow = xraw_flat[:, 0:2 * ROW].rearrange("p (q d) -> p q d", q=2)
        xb2 = xraw_flat[:, 2 * ROW:4 * ROW].rearrange("p (q d) -> p q d", q=2)
        o_t = sg[:, 0, :].rearrange("p (q d) -> p q d", q=2)
        r2 = xtok[:, 0, 0:2, :]
        stats2 = sb("stats2", [P, 6])
        mv2 = sb("mv2", [P, 2])
        std2 = sb("std2", [P, 1])
        rstd2 = sb("rstd2", [P, 1])
        idx2 = sb("idx2", [P, 2], I32)

        bank = [ctx.enter_context(nc.psum_tensor(f"bank{i}", [P, 512], F32)) for i in range(8)]
        CONV0, GATE0, SMALL, SSM, OUT0 = 0, 2, 4, 5, 6
        HID0, HIDT0, XGT, Y0 = 0, 2, 4, 6
        R0, RK = 0, 64

        in_small, in_win, in_wx, in_wout = sem("in_small"), sem("in_win"), sem("in_wx"), sem("in_wout")
        in_x = [sem("in_x0"), sem("in_x1")]
        in_tok = [sem("in_tok0"), sem("in_tok1")]
        in_w01 = sem("in_w01")
        in_w, in_b, in_row = sem("in_w"), sem("in_b"), [sem("in_row0"), sem("in_row1")]
        rows_out = [sem("rows_out0"), sem("rows_out1")]
        fill_out, y_out = sem("fill_out"), [sem("y_out0"), sem("y_out1")]
        const_p, const_v, aexp_s, aneg_s = sem("const_p"), sem("const_v"), sem("aexp_s"), sem("aneg_s")
        whi, wlo = sem("whi"), sem("wlo")
        conv_mm, gate_mm, ssm_mm, x1T_mm = sem("conv_mm"), sem("gate_mm"), sem("ssm_mm"), sem("x1T_mm")
        logit_mm, rank_mm, xdbl_mm, out_mm = sem("logit_mm"), sem("rank_mm"), sem("xdbl_mm"), sem("out_mm")
        hid_mm, hT_mm, xg_mm, y_mm = sem("hid_mm"), sem("hT_mm"), sem("xg_mm"), sem("y_mm")
        cin_done, halo_done, cv_done, cvhi = sem("cin_done"), sem("halo_done"), sem("cv_done"), sem("cvhi")
        sg_done, gohi, xhi, x1T_done, sp_step = sem("sg_done"), sem("gohi"), sem("xhi"), sem("x1T_done"), sem("sp_step")
        hThi, xghi, std_s, ehi = sem("hThi"), sem("xghi"), sem("std_s"), sem("ehi")
        tap, norm, route, onehot = sem("tap"), sem("norm"), sem("route"), sem("onehot")
        posd, skip, go = sem("posd"), sem("skip"), sem("go")
        scan_s, resd, statd, mvd = sem("scan_s"), sem("resd"), sem("statd"), sem("mvd")
        tabs, tab_ready = sem("tabs"), sem("tab_ready")
        fills = sem("fills")
        evac, hTlo, xglo, r_s, ln2, o_s = sem("evac"), sem("hTlo"), sem("xglo"), sem("r_s"), sem("ln2"), sem("o_s")
        cvlo, xlo, golo, rstd_s, xb2_s, elo = sem("cvlo"), sem("xlo"), sem("golo"), sem("rstd_s"), sem("xb2_s"), sem("elo")
        base_set = sem("base_set")
        cps, rec = sem("cps"), sem("rec")

        TAPN = KI * (TAPS - 1)
        ROUTE = 8
        SCAN, SOFT = 5, 4
        PIECES, PIECE = 4, 1024

        def piece(e_buf, part, i):
            at = (i // 2) * WHALF + part * W1N + (i % 2) * PIECE
            return wsp[:, e_buf, at:at + PIECE]

        def known(eng, value):
            return value if isinstance(value, int) else eng.to_reg(value)

        def late(g):
            return not (isinstance(g, int) and g == 0)

        block = ctx.enter_context(nc.Block())

        def phase1(eng, step):
            step(0, 0, "A")
            step(0, 1, "AB")
            with eng.Fori(1, NCH // 2) as g:
                step(g, 0, "ABC")
                step(g, 1, "ABC")
            step(NCH // 2, 0, "BC")
            step(NCH // 2, 1, "C")

        def phase2(eng, slot):
            slot(0, 0, "F")
            slot(0, 1, "FG")
            slot(1, 0, "FGT")
            slot(1, 1, "FGTS")
            with eng.Fori(2, SLOTS // 2) as g:
                slot(g, 0, "FGTS")
                slot(g, 1, "FGTS")
            slot(SLOTS // 2, 0, "FGTS")
            slot(SLOTS // 2, 1, "GTS")
            slot(SLOTS // 2 + 1, 0, "TS")
            slot(SLOTS // 2 + 1, 1, "S")

        xT_v = xT.rearrange("(k p) t -> p k t", p=P)
        x_v = x.rearrange("(c j p) d -> c p j d", j=SUB, p=P)

        def load_expert(eng, e, landed):
            eng.dma_start(wraw[:, 0:W1N].rearrange("p (k f) -> p k f", k=KD),
                          w1[e].rearrange("(k p) f -> p k f", p=P)).then_inc(landed, 16)
            eng.dma_start(wraw[:, W1N:2 * W1N].rearrange("p (b d) -> p b d", b=KF),
                          w2[e].rearrange("(b p) d -> p b d", p=P)).then_inc(landed, 16)

        def load_bias(eng, e, v, landed):
            eng.dma_start(b1b[:, v, :], b1[e].partition_broadcast(P)).then_inc(landed, 16)
            eng.dma_start(b2b[:, v, 0:DM], b2[e].partition_broadcast(P)).then_inc(landed, 16)


        @block.sync
        def _(sp):
            sp.dma_start(xraw[:, 0, :, :], xT_v[:, :, 0:CH]).then_inc(in_x[0], 16)
            sp.dma_start(win_raw.rearrange("p (k n) -> p k n", k=KD), w_in.rearrange("(k p) n -> p k n", p=P)).then_inc(in_win, 16)
            sp.dma_start(cw[:, :, :], conv_w.rearrange("(k p) w -> p k w", p=P)).then_inc(in_small, 16)
            sp.dma_start(cb[:, :], conv_b).then_inc(in_small, 16)
            sp.dma_start(dp[:, :], d_par).then_inc(in_small, 16)
            sp.dma_start(alog[:, :], a_log.rearrange("(n a) -> n a", a=1)).then_inc(in_small, 16)
            sp.dma_start(wr_s[:, :, :], wr.rearrange("(k p) e -> p k e", p=P)).then_inc(in_small, 16)
            sp.dma_start(br_s[:, :], br.partition_broadcast(P)).then_inc(in_small, 16)
            sp.dma_start(wx_raw.rearrange("p (k n) -> p k n", k=KI), w_x.rearrange("(k p) n -> p k n", p=P)).then_inc(in_wx, 16)
            sp.dma_start(wout_raw.rearrange("p (k n) -> p k n", k=KI), w_out.rearrange("(k p) n -> p k n", p=P)).then_inc(in_wout, 16)
            sp.dma_start(xtok[:, 0, :, :], x_v[0]).then_inc(in_tok[0], 16)

            def step(g, u, stages):
                it = 2 * g + u
                if "A" not in stages:
                    return
                start = isinstance(g, int)
                if not (start and u == 0):
                    sp.wait_ge(xhi, KD * it)
                    sp.wait_ge(xlo, KD * it)
                nxt = it + 1 if start else (it + 1) % NCH
                sp.dma_start(xraw[:, 1 - u, :, :], xT_v[:, :, bass.ds(nxt * CH, CH)]).then_inc(in_x[1 - u], 16)
                if start and u == 0:
                    sp.wait_ge(whi, 4)
                    sp.wait_ge(wlo, 4)
                    load_expert(sp, 0, in_w01)
                    return
                if not start:
                    sp.wait_ge(norm, SUB * (it - 1))
                sp.dma_start(xtok[:, u, :, :], x_v[it]).then_inc(in_tok[u], 16)

            phase1(sp, step)
            sp.wait_ge(ehi, PIECES)
            sp.wait_ge(elo, PIECES)
            load_expert(sp, 1, in_w01)
            sp.wait_ge(tab_ready, 1)
            for q in range(2):
                sp.wait_ge(rows_out[q], 16 * (SUB * NCH // 2 + 1))
            sp.wait_ge(fill_out, 16 * NE)

            def load_row(j, q):
                r0 = sp.value_load(tab[0:1, T_ROW, bass.ds(j, 1)], min_val=0, max_val=FILL_ROW0)
                sp.dma_start(xrow[:, q, :], rows[bass.ds(r0, P), :]).then_inc(in_row[q], 16)

            sp.wait_ge(xlo, KD * (NCH + 1))
            sp.wait_ge(xhi, KD * (NCH + 1))
            load_row(0, 0)
            load_row(1, 1)
            with sp.Fori(1, SLOTS // 2 + 1) as g:
                for u in range(2):
                    j = 2 * g + u
                    sp.wait_ge(xb2_s, j - 1)
                    sp.wait_ge(xg_mm, j - 1)
                    load_row(j, u)

        @block.gpsimd
        def _(pool):
            pool.memset(ident[:, :], 0.0).then_inc(cps, 1)
            pool.memset(tri[:, :], 1.0).then_inc(cps, 1)
            pool.iota(ebase[:, :], pattern=[[REGION, NE]], base=0, channel_multiplier=0,
                      allow_small_or_imprecise_dtypes=True).then_inc(cps, 1)
            pool.iota(base[:, 0, :], pattern=[[REGION, NE]], base=0, channel_multiplier=0,
                      allow_small_or_imprecise_dtypes=True).then_inc(base_set, 1)
            pool.iota(first_w[:, :], pattern=[[-1, NE]], base=NE, channel_multiplier=0,
                      allow_small_or_imprecise_dtypes=True)
            pool.iota(slot_no[:, :], pattern=[[1, NTAB]], base=0, channel_multiplier=0,
                      allow_small_or_imprecise_dtypes=True)
            pool.iota(fill_no[:, :], pattern=[[1, 1]], base=0, channel_multiplier=1,
                      allow_small_or_imprecise_dtypes=True)
            for q in range(2):
                pool.iota(x1row[:, q, :, DM:ROW], pattern=[[P, SUB], [1, 1]], base=(q - 2) * CH,
                          channel_multiplier=1, allow_small_or_imprecise_dtypes=True)
            pool.wait_ge(fills, 2)
            for q in range(2):
                pool.dma_start(rows[FILL_ROW0 + q * P // 2:FILL_ROW0 + (q + 1) * P // 2, :],
                               fill[q * P // 2:(q + 1) * P // 2, :]).then_inc(rows_out[q], 16)
            pool.wait_ge(cps, 2)
            pool.affine_select(out=ident[:, :], in_=ident[:, :], compare_op=ALU.not_equal, fill=1.0,
                               base=0, pattern=[[-1, P]], channel_multiplier=1)
            pool.affine_select(out=tri[:, :], in_=tri[:, :], compare_op=ALU.is_gt, fill=0.0,
                               base=0, pattern=[[1, P]], channel_multiplier=-1).then_inc(const_p, 1)
            for k in range(KD):
                pool.wait_ge(xhi, k + 1)
                pool.tensor_tensor(xs[:, 0, 1, k, :], xraw[:, 0, k, :], xs[:, 0, 0, k, :].bitcast(F32),
                                   ALU.subtract).then_inc(xlo, 1)

            def step(g, u, stages):
                it = 2 * g + u
                if "A" in stages:
                    for b in range(KI):
                        pool.wait_ge(cvhi, KI * it + b + 1)
                        pool.tensor_tensor(cvs[:, 1, b, :], cv[:, u, b, :], cvs[:, 0, b, :].bitcast(F32),
                                           ALU.subtract).then_inc(cvlo, 1)
                    for k in range(KD):
                        pool.wait_ge(xhi, KD * (it + 1) + k + 1)
                        pool.tensor_tensor(xs[:, 1 - u, 1, k, :], xraw[:, 1 - u, k, :],
                                           xs[:, 1 - u, 0, k, :].bitcast(F32), ALU.subtract).then_inc(xlo, 1)
                if "B" in stages:
                    for b in range(KI):
                        pool.wait_ge(gohi, KI * (it - 1) + b + 1)
                        pool.tensor_tensor(gos[:, 1, b, :], cv[:, 1 - u, b, :], gos[:, 0, b, :].bitcast(F32),
                                           ALU.subtract).then_inc(golo, 1)
                if "C" in stages:
                    pool.wait_ge(const_v, 1)
                    pool.wait_ge(norm, SUB * (it - 1))
                    pool.wait_ge(posd, it - 1)
                    for j in range(SUB):
                        pool.indirect_dma_start(
                            rows, bass.IndirectOffsetOnAxis(ap=posi[:, u, j:j + 1], axis=0),
                            x1row[:, u, j, :], None).then_inc(rows_out[u], 16)
                if "B" in stages:
                    pool.wait_ge(const_v, 1)
                    pool.wait_ge(mvd, SUB * it)
                    pool.tensor_scalar(ve[:, :], mv[:, :, 1], EPS, None, ALU.add).then_inc(rstd_s, 1)
                    pool.wait_ge(rstd_s, 2 * it - 1)
                    pool.tensor_tensor(rstd[:, :], ve[:, :], half[:, :], ALU.pow).then_inc(rstd_s, 1)

            phase1(pool, step)
            pool.wait_ge(tap, TAPN * NCH)
            pool.wait_ge(halo_done, NCH)
            load_bias(pool, 0, 0, in_b)
            pool.wait_ge(fills, 3)
            for e in range(NE):
                pool.indirect_dma_start(rows, bass.IndirectOffsetOnAxis(ap=filli[:, e:e + 1], axis=0),
                                        fill[:, :], None).then_inc(fill_out, 16)

            def split_lo(e, buf):
                for i in range(PIECES):
                    pool.wait_ge(ehi, PIECES * e + i + 1)
                    pool.tensor_tensor(piece(buf, 1, i), wraw[:, i * PIECE:(i + 1) * PIECE],
                                       piece(buf, 0, i).bitcast(F32), ALU.subtract).then_inc(elo, 1)

            split_lo(0, 0)
            pool.wait_ge(tab_ready, 1)
            pool.wait_ge(const_v, 2)

            def slot(g, u, stages):
                j = 2 * g + u
                if "S" in stages:
                    done = known(pool, j - 2)
                    pool.wait_ge(tab_ready, 1)
                    pool.wait_ge(o_s, done)
                    pool.indirect_dma_start(out, bass.IndirectOffsetOnAxis(ap=idx2[:, 1 - u:2 - u], axis=0),
                                            o_t[:, 1 - u, :], None, bounds_check=TOKENS - 1,
                                            oob_is_err=False).then_inc(y_out[1 - u], 16)
                if "F" not in stages:
                    return
                e = pool.value_load(tab[0:1, T_E, bass.ds(j, 1)], min_val=0, max_val=NE - 1)
                v = pool.value_load(tab[0:1, T_BUF, bass.ds(j, 1)], min_val=0, max_val=1)
                pool.wait_ge(in_b, 32 * (e + 1))
                pool.wait_ge(in_row[u], 16 * (g + 1))
                if late(g):
                    pool.wait_ge(r_s, j - 1)
                pool.tensor_tensor(xb2[:, u, :], xrow[:, u, :], b2b[:, v, :], ALU.add).then_inc(xb2_s, 1)

                def next_expert(e, nv):
                    split_lo(e + 1, nv)
                    load_bias(pool, (e + 1) % NE, nv, in_b)
                    pool.wait_ge(elo, PIECES * (e + 2))
                    if isinstance(e, int):
                        load_expert(pool, e + 2, in_w)
                    else:
                        load_expert(pool, (e + 2) % NE, in_w)

                if isinstance(g, int) and j == 0:
                    next_expert(0, 1)
                else:
                    first = pool.value_load(tab[0:1, T_FIRST, bass.ds(j, 1)], min_val=0, max_val=1)
                    nv = pool.value_load(tab[0:1, T_NEXTBUF, bass.ds(j, 1)], min_val=0, max_val=1)
                    with pool.If(first == 1):
                        next_expert(e, nv)

            phase2(pool, slot)
            for q in range(2):
                pool.wait_ge(y_out[q], 16 * ((SLOTS + 1 - q) // 2))
            pool.wait_ge(in_w, 32 * (NE - 1))
            pool.wait_ge(in_row[1], 16 * ((NTAB) // 2))

        @block.scalar
        def _(act):
            act.wait_ge(in_x[0], 16)
            for k in range(KD):
                act.activation(xs[:, 0, 0, k, :], xraw[:, 0, k, :], ACT.Copy).then_inc(xhi, 1)
            act.wait_ge(in_win, 16)
            win_r = win_raw.rearrange("p (k n) -> p k n", k=KD)
            for n in range(2):
                act.activation(win[:, 0, :, n * DI:(n + 1) * DI], win_r[:, :, n * DI:(n + 1) * DI],
                               ACT.Copy).then_inc(whi, 1)
            act.wait_ge(in_wx, 16)
            act.activation(wx[:, 0, :, :], wx_raw.rearrange("p (k n) -> p k n", k=KI), ACT.Copy).then_inc(whi, 1)
            act.wait_ge(in_wout, 16)
            act.activation(wout[:, 0, :, :], wout_raw.rearrange("p (k n) -> p k n", k=KI), ACT.Copy).then_inc(whi, 1)
            act.wait_ge(in_small, 96)
            act.activation(aexp[:, :], alog[:, :], ACT.Exp).then_inc(aexp_s, 1)
            act.wait_ge(aneg_s, 1)

            def step(g, u, stages):
                it = 2 * g + u
                if "A" in stages:
                    for b in range(KI):
                        act.wait_ge(conv_mm, KI * it + b + 1)
                        if b == 0 and late(g):
                            act.wait_ge(tap, TAPN * (it - 1))
                        if b == 0 and (late(g) or u):
                            act.wait_ge(cv_done, KI * it)
                        act.activation(cin[:, u, b, TAPS - 1:], bank[CONV0 + b % 2][:, :], ACT.Copy)
                        act.activation(acc[:, b, :], bank[CONV0 + b % 2][:, :], ACT.Identity,
                                       bias=cb[:, b:b + 1], scale=cw[:, b, TAPS - 1:TAPS]).then_inc(cin_done, 1)
                    if late(g) or u:
                        act.wait_ge(tap, TAPN * it)
                    act.wait_ge(cin_done, KI * (it + 1))
                    act.activation(cin[:, 1 - u, :, 0:TAPS - 1], cin[:, u, :, CH:], ACT.Copy).then_inc(halo_done, 1)
                if "C" in stages:
                    for k in range(KD):
                        act.wait_ge(x1T_mm, KD * (it - 2) + k + 1)
                        act.activation(x1T[:, k, :], bank[GATE0 + k][:, :], ACT.Copy).then_inc(x1T_done, 1)
                if "A" in stages:
                    def high(b):
                        act.wait_ge(cv_done, KI * it + b + 1)
                        if b == 0 and (late(g) or u):
                            act.wait_ge(xdbl_mm, it)
                        act.activation(cvs[:, 0, b, :], cv[:, u, b, :], ACT.Copy).then_inc(cvhi, 1)

                    for b in range(KI):
                        act.wait_ge(tap, TAPN * it + (TAPN // 2) * (b // 2) + 5 + b % 2)
                        if b == 0 and late(g):
                            act.wait_ge(golo, KI * (it - 1))
                            act.wait_ge(gohi, KI * (it - 1))
                        act.activation(cv[:, u, b, :], acc[:, b, :], ACT.Silu).then_inc(cv_done, 1)
                        if b:
                            high(b - 1)
                    high(KI - 1)
                if "B" in stages:
                    for b in range(KI):
                        act.wait_ge(gate_mm, KI * (it - 1) + b + 1)
                        if b == 0:
                            if late(g):
                                act.wait_ge(go, KI * (it - 1))
                        act.activation(sg[:, b, :], bank[GATE0 + b % 2][:, :], ACT.Silu).then_inc(sg_done, 1)
                if "A" in stages:
                    act.wait_ge(in_x[1 - u], 16 * (g + 1 + u))
                    if late(g) or u:
                        act.wait_ge(gate_mm, KI * it)
                    for k in range(KD):
                        act.activation(xs[:, 1 - u, 0, k, :], xraw[:, 1 - u, k, :], ACT.Copy).then_inc(xhi, 1)
                if "B" in stages:
                    for b in range(KI):
                        act.wait_ge(go, KI * (it - 1) + b + 1)
                        if b == 0 and late(g):
                            act.wait_ge(out_mm, SUB * (it - 1))
                        act.activation(gos[:, 0, b, :], cv[:, 1 - u, b, :], ACT.Copy).then_inc(gohi, 1)
                if "A" in stages:
                    act.wait_ge(xdbl_mm, it + 1)
                    act.activation(soft[:, :], bank[SMALL][0:NST, :], ACT.Abs).then_inc(sp_step, 1)
                    act.wait_ge(sp_step, SOFT * it + 1)
                    act.activation(soft[:, :], soft[:, :], ACT.Exp, scale=-1.0).then_inc(sp_step, 1)
                    act.wait_ge(sp_step, SOFT * it + 2)
                    act.activation(soft[:, :], soft[:, :], ACT.Ln, bias=1.0).then_inc(sp_step, 1)
                    act.wait_ge(scan_s, SCAN * it + 1)
                    act.activation(dA[:, :], delta[:, :], ACT.Exp, scale=aneg[:, 0:1]).then_inc(sp_step, 1)

            phase1(act, step)
            def split_hi(i, buf):
                act.activation(piece(buf, 0, i), wraw[:, i * PIECE:(i + 1) * PIECE], ACT.Copy).then_inc(ehi, 1)

            act.wait_ge(in_w01, 32)
            for i in range(PIECES):
                if i == PIECES // 2:
                    act.wait_ge(out_mm, SUB * NCH)
                split_hi(i, 0)
            act.wait_ge(tab_ready, 1)

            def x_hi(j, q):
                act.wait_ge(xg_mm, j + 1)
                act.activation(xg[:, q, 0, :, :], bank[XGT][:, 0:DM].rearrange("p (k t) -> p k t", k=KD),
                               ACT.Copy).then_inc(xghi, 1)

            def relu_hi(n, half_no):
                act.wait_ge(hT_mm, n)
                act.activation(hT[:, 0, 4 * half_no:4 * half_no + 4, :],
                               bank[HIDT0 + half_no][:, :].rearrange("p (b t) -> p b t", b=4), ACT.Relu).then_inc(hThi, 1)

            act.wait_ge(out_mm, SUB * NCH)
            x_hi(0, 0)

            def slot(g, u, stages):
                j = 2 * g + u
                if "G" in stages:
                    relu_hi(2 * j, 1)
                if "T" in stages:
                    act.wait_ge(ln2, 2 * (j - 1))
                    act.activation(std2[:, :], mv2[:, 1:2], ACT.Sqrt, bias=eps_t[:, 0:1]).then_inc(std_s, 1)
                if "F" in stages:
                    x_hi(j + 1, 1 - u)
                    relu_hi(2 * j + 1, 0)

                    if isinstance(g, int) and j == 0:
                        act.wait_ge(in_w01, 64)
                        for i in range(PIECES):
                            split_hi(i, 1)
                    else:
                        e = act.value_load(tab[0:1, T_E, bass.ds(j, 1)], min_val=0, max_val=NE - 1)
                        first = act.value_load(tab[0:1, T_FIRST, bass.ds(j, 1)], min_val=0, max_val=1)
                        nv = act.value_load(tab[0:1, T_NEXTBUF, bass.ds(j, 1)], min_val=0, max_val=1)
                        with act.If(first == 1):
                            act.wait_ge(y_mm, j)
                            act.wait_ge(in_w, 32 * e)
                            for i in range(PIECES):
                                split_hi(i, nv)

            phase2(act, slot)

        @block.vector
        def _(dve):
            dve.memset(ones[:, :], 1.0)
            dve.memset(ones16[:, :], 1.0)
            dve.memset(eps_t[:, :], EPS)
            dve.memset(half[:, :], -0.5)
            dve.memset(fill[:, :], 0.0).then_inc(fills, 1)
            dve.memset(cin[:, 0, :, 0:TAPS - 1], 0.0).then_inc(const_v, 1)
            dve.wait_ge(fills, 1)
            dve.memset(fill[:, DM:ROW], FILL_ID).then_inc(fills, 1)
            win_r = win_raw.rearrange("p (k n) -> p k n", k=KD)
            for n in range(2):
                dve.wait_ge(whi, n + 1)
                dve.tensor_tensor(win[:, 1, :, n * DI:(n + 1) * DI], win_r[:, :, n * DI:(n + 1) * DI],
                                  win[:, 0, :, n * DI:(n + 1) * DI].bitcast(F32), ALU.subtract).then_inc(wlo, 1)
            dve.wait_ge(whi, 3)
            dve.tensor_tensor(wx[:, 1, :, :], wx_raw.rearrange("p (k n) -> p k n", k=KI),
                              wx[:, 0, :, :].bitcast(F32), ALU.subtract).then_inc(wlo, 1)
            dve.wait_ge(whi, 4)
            dve.tensor_tensor(wout[:, 1, :, :], wout_raw.rearrange("p (k n) -> p k n", k=KI),
                              wout[:, 0, :, :].bitcast(F32), ALU.subtract).then_inc(wlo, 1)
            dve.wait_ge(aexp_s, 1)
            dve.tensor_scalar(aneg[:, :], aexp[:, :], -1.0, None, ALU.mult).then_inc(aneg_s, 1)
            dve.wait_ge(in_small, 96)
            dve.wait_ge(cps, 3)
            dve.wait_ge(const_p, 1)

            def step(g, u, stages):
                it = 2 * g + u
                A, B, C = "A" in stages, "B" in stages, "C" in stages
                rc = ROUTE * (it - 2)

                def taps(p):
                    for w in (2, 1, 0):
                        for b in (2 * p, 2 * p + 1):
                            n = TAPN * it + 6 * p + 2 * (2 - w) + b % 2
                            if w == 2:
                                dve.wait_ge(cin_done, KI * it + b + 1)
                                if b == 0 and (late(g) or u):
                                    dve.wait_ge(halo_done, it)
                            else:
                                dve.wait_ge(tap, n - 1)
                            dve.scalar_tensor_tensor(acc[:, b, :], cin[:, u, b, w:w + CH], cw[:, b, w:w + 1],
                                                     acc[:, b, :], ALU.mult, ALU.add).then_inc(tap, 1)

                def normalise():
                    dve.wait_ge(rstd_s, 2 * (it - 1))
                    dve.wait_ge(rows_out[u], 16 * SUB * (g - 1) + 16)
                    dve.tensor_scalar(x1row[:, u, :, DM:ROW], x1row[:, u, :, DM:ROW], float(2 * CH), None, ALU.add)
                    for j in range(SUB):
                        dve.tensor_scalar(x1row[:, u, j, 0:DM], xtok[:, u, j, :], mv[:, j, 0:1], rstd[:, j:j + 1],
                                          ALU.subtract, ALU.mult).then_inc(norm, 1)

                def route1(n):
                    if n == 0:
                        dve.wait_ge(logit_mm, it - 1)
                        dve.tensor_tensor(lg[:, :, :], bank[SMALL][:, R0:R0 + SUB * NE].rearrange("p (j e) -> p j e", e=NE),
                                          br_s[:, :].unsqueeze(1).to_broadcast([P, SUB, NE]), ALU.add).then_inc(route, 1)
                        return
                    dve.wait_ge(route, rc + n)
                    if n == 1:
                        dve.tensor_reduce(mx[:, :], lg[:, :, :], AX_X, ALU.max).then_inc(route, 1)
                    elif n == 2:
                        dve.tensor_tensor(eq[:, :, :], lg[:, :, :], mx[:, :].unsqueeze(2).to_broadcast([P, SUB, NE]),
                                          ALU.is_ge).then_inc(route, 1)
                    elif n == 3:
                        dve.tensor_tensor(ew[:, :, :], eq[:, :, :], first_w[:, :].unsqueeze(1).to_broadcast([P, SUB, NE]),
                                          ALU.mult).then_inc(route, 1)
                    elif n == 4:
                        dve.tensor_reduce(m2[:, :], ew[:, :, :], AX_X, ALU.max).then_inc(route, 1)
                    elif n == 5:
                        dve.tensor_tensor(oh[:, :, :], ew[:, :, :], m2[:, :].unsqueeze(2).to_broadcast([P, SUB, NE]),
                                          ALU.is_equal).then_inc(onehot, 1)

                def route2(n):
                    if n == 0:
                        dve.wait_ge(rank_mm, it - 1)
                        dve.wait_ge(base_set, it - 1)
                        dve.tensor_tensor(p2[:, :, :], bank[SMALL][:, RK:RK + SUB * NE].rearrange("p (j e) -> p j e", e=NE),
                                          base[:, u, :].unsqueeze(1).to_broadcast([P, SUB, NE]), ALU.add).then_inc(route, 1)
                        dve.tensor_tensor(base[:, 1 - u, :], base[:, u, :],
                                          bank[SMALL][:, RK + SUB * NE:RK + (SUB + 1) * NE], ALU.add).then_inc(base_set, 1)
                        return
                    dve.wait_ge(route, rc + 5 + n)
                    if n == 1:
                        dve.wait_ge(onehot, it - 1)
                        dve.tensor_tensor(p3[:, :, :], p2[:, :, :], oh[:, :, :], ALU.mult).then_inc(route, 1)
                    elif n == 2:
                        dve.tensor_reduce(posf[:, :], p3[:, :, :], AX_X, ALU.add).then_inc(route, 1)
                    elif n == 3:
                        dve.tensor_copy(posi[:, u, :], posf[:, :]).then_inc(posd, 1)

                def skip_path(b):
                    if b == 0:
                        dve.wait_ge(ssm_mm, it)
                        dve.wait_ge(cvhi, KI * it)
                        dve.wait_ge(cvlo, KI * it)
                    dve.scalar_tensor_tensor(cv[:, 1 - u, b, :], cv[:, 1 - u, b, :], dp[:, b:b + 1],
                                             bank[SSM][:, :], ALU.mult, ALU.add).then_inc(skip, 1)

                def gate(b):
                    dve.wait_ge(skip, KI * (it - 1) + b + 1)
                    dve.wait_ge(sg_done, KI * (it - 1) + b + 1)
                    dve.tensor_tensor(cv[:, 1 - u, b, :], cv[:, 1 - u, b, :], sg[:, b, :], ALU.mult).then_inc(go, 1)

                def residual(j):
                    dve.wait_ge(out_mm, SUB * (it - 1) + j + 1)
                    if j == 0:
                        dve.wait_ge(in_tok[1 - u], 16 * (g + u))
                    dve.tensor_tensor(xtok[:, 1 - u, j, :], bank[OUT0 + j % 2][:, 0:DM], xtok[:, 1 - u, j, :],
                                      ALU.add).then_inc(resd, 1)

                def stat(j):
                    dve.wait_ge(resd, SUB * (it - 1) + j + 1)
                    dve.bn_stats(stats[:, j, :], xtok[:, 1 - u, j, :]).then_inc(statd, 1)

                def aggregate(j):
                    done = known(dve, SUB * (it - 1) + j + 1)
                    dve.wait_ge(const_v, 1)
                    dve.wait_ge(statd, done)
                    dve.bn_aggr(mv[:, j, :], stats[:, j, :]).then_inc(mvd, 1)

                def scan(n):
                    if n == 0:
                        dve.wait_ge(sp_step, SOFT * it + 3)
                        dve.scalar_tensor_tensor(delta[:, :], bank[SMALL][0:NST, :], 0.0, soft[:, :],
                                                 ALU.max, ALU.add).then_inc(scan_s, 1)
                        return
                    dve.wait_ge(scan_s, SCAN * it + n)
                    if n == 1:
                        if late(g) or u:
                            dve.wait_ge(ssm_mm, it)
                        dve.tensor_tensor(dB[:, :], delta[:, :], bank[SMALL][B_ROW:B_ROW + NST, :], ALU.mult).then_inc(scan_s, 1)
                    elif n == 2:
                        dve.wait_ge(cv_done, KI * it + 1)
                        dve.tensor_tensor(dB[:, :], dB[:, :], cv[0:NST, u, 0, :], ALU.mult).then_inc(scan_s, 1)
                    elif n == 3:
                        dve.wait_ge(sp_step, SOFT * it + 4)
                        h0 = hst[:, 1 - u, CH - 1:CH] if late(g) or u else 0.0
                        dve.tensor_tensor_scan(hst[:, u, :], dA[:, :], dB[:, :], h0, ALU.mult, ALU.add).then_inc(scan_s, 1)
                    elif n == 4:
                        dve.tensor_tensor(dB[:, :], hst[:, u, :], bank[SMALL][C_ROW:C_ROW + NST, :], ALU.mult).then_inc(scan_s, 1)

                if A:
                    taps(0)
                if C:
                    normalise()
                if A:
                    taps(1)
                if B:
                    skip_path(0)
                    skip_path(1)
                if C:
                    route1(0)
                if B:
                    skip_path(2)
                if C:
                    route1(1)
                if B:
                    skip_path(3)
                if C:
                    route1(2)
                if B:
                    gate(0)
                if C:
                    route1(3)
                if B:
                    gate(1)
                if C:
                    route1(4)
                if B:
                    gate(2)
                if C:
                    route1(5)
                if B:
                    gate(3)
                if C:
                    for n in range(4):
                        route2(n)
                if B:
                    residual(0)
                    residual(1)
                    stat(0)
                if A:
                    scan(0)
                if B:
                    stat(1)
                if A:
                    scan(1)
                if B:
                    residual(2)
                if A:
                    scan(2)
                if B:
                    stat(2)
                    aggregate(0)
                if A:
                    scan(3)
                if B:
                    residual(3)
                    aggregate(1)
                if A:
                    scan(4)
                if B:
                    stat(3)
                    aggregate(2)
                    aggregate(3)

            phase1(dve, step)

            tn = [0]

            def chain(ins):
                tn[0] += 1
                ins.then_inc(tabs, 1)
                dve.wait_ge(tabs, tn[0])

            dve.wait_ge(base_set, NCH + 1)
            chain(dve.tensor_scalar(fillf[:, :], base[:, 0, :], fill_no[:, 0:1], None, ALU.add))
            dve.tensor_copy(filli[:, :], fillf[:, :]).then_inc(fills, 1)
            chain(dve.tensor_tensor(cnt[:, :], base[0:1, 0, :], ebase[0:1, :], ALU.subtract))
            chain(dve.tensor_scalar(cnti[:, :], cnt[:, :], float(P - 1), None, ALU.add))
            chain(dve.tensor_scalar(cnts[:, :], cnti[:, :], 7, None, ALU.logical_shift_right))
            chain(dve.tensor_copy(ntf[:, :], cnts[:, :]))
            chain(dve.tensor_scalar(nt[:, :], ntf[:, :], 1.0, None, ALU.max))
            chain(dve.tensor_tensor_scan(end[:, :], ones16[0:1, 0:NE], nt[:, :], 0.0, ALU.mult, ALU.add))
            chain(dve.tensor_tensor(past[:, :, :], end[:, :].unsqueeze(1).to_broadcast([1, NTAB, NE]),
                                    slot_no[:, :].unsqueeze(2).to_broadcast([1, NTAB, NE]), ALU.is_le))
            chain(dve.tensor_reduce(ej[:, :], past[:, :, :], AX_X, ALU.add))
            chain(dve.tensor_tensor(pastn[:, :, :], past[:, :, :], nt[:, :].unsqueeze(1).to_broadcast([1, NTAB, NE]), ALU.mult))
            chain(dve.tensor_reduce(sj[:, :], pastn[:, :, :], AX_X, ALU.add))
            chain(dve.tensor_tensor(dj[:, :], slot_no[:, :], sj[:, :], ALU.subtract))
            chain(dve.tensor_scalar(dj[:, :], dj[:, :], float(P), None, ALU.mult))
            chain(dve.scalar_tensor_tensor(rj[:, :], ej[:, :], float(REGION), dj[:, :], ALU.mult, ALU.add))
            chain(dve.tensor_scalar(rj[:, :], rj[:, :], float(FILL_ROW0), None, ALU.min))
            dve.tensor_copy(tab[:, T_ROW, :], rj[:, :])
            chain(dve.tensor_scalar(e7[:, :], ej[:, :], float(NE - 1), None, ALU.min))
            chain(dve.tensor_copy(tab[:, T_E, :], e7[:, :]))
            chain(dve.tensor_scalar(tab[:, T_BUF, :], tab[:, T_E, :], 1, None, ALU.bitwise_and))
            dve.tensor_scalar(tab[:, T_NEXTBUF, :], tab[:, T_BUF, :], 1, None, ALU.bitwise_xor)
            chain(dve.memset(fj[:, 0:1], 1.0))
            chain(dve.tensor_tensor(fj[:, 1:], e7[:, 1:], e7[:, :-1], ALU.not_equal))
            chain(dve.scalar_tensor_tensor(fj[:, :], e7[:, :], float(NE - 1), fj[:, :], ALU.is_lt, ALU.mult))
            dve.tensor_copy(tab[:, T_FIRST, :], fj[:, :]).then_inc(tab_ready, 1)
            dve.wait_ge(tab_ready, 1)
            dve.wait_ge(halo_done, NCH)
            dve.memset(b2b[:, :, DM:ROW], 0.0).then_inc(const_v, 1)

            def x_lo(j, q):
                dve.wait_ge(xghi, j + 1)
                dve.tensor_tensor(xg[:, q, 1, :, :], bank[XGT][:, 0:DM].rearrange("p (k t) -> p k t", k=KD),
                                  xg[:, q, 0, :, :].bitcast(F32), ALU.subtract).then_inc(xglo, 1)

            def relu_lo(n, half_no):
                s = 4 * half_no
                dve.wait_ge(hThi, n)
                dve.scalar_tensor_tensor(hT[:, 1, s:s + 4, :].rearrange("p b t -> p (b t)"), bank[HIDT0 + half_no][:, :], 0.0,
                                         hT[:, 0, s:s + 4, :].rearrange("p b t -> p (b t)").bitcast(F32),
                                         ALU.max, ALU.subtract).then_inc(hTlo, 1)

            x_lo(0, 0)

            def slot(g, u, stages):
                j = 2 * g + u
                F, G, T = "F" in stages, "G" in stages, "T" in stages
                if F:
                    e = dve.value_load(tab[0:1, T_E, bass.ds(j, 1)], min_val=0, max_val=NE - 1)
                    v = dve.value_load(tab[0:1, T_BUF, bass.ds(j, 1)], min_val=0, max_val=1)

                def bias(half_no):
                    dve.wait_ge(hid_mm, 2 * j + half_no + 1)
                    if half_no == 0:
                        dve.wait_ge(in_b, 32 * (e + 1))
                        if late(g) or u:
                            dve.wait_ge(hT_mm, 2 * j - 1)
                    dve.tensor_tensor(h[:, half_no, :], bank[HID0 + half_no][:, :],
                                      b1b[:, v, half_no * 512:(half_no + 1) * 512], ALU.add).then_inc(evac, 1)

                if T:
                    dve.wait_ge(xb2_s, j - 1)
                    dve.wait_ge(y_mm, j - 1)
                    if not isinstance(g, int) or g > 1:
                        dve.wait_ge(y_out[u], 16 * (g - 1))
                    dve.tensor_copy(idx2[:, u:u + 1], xb2[:, u, DM:ROW])
                    dve.tensor_tensor(r2[:, u, :], bank[Y0 + u][:, 0:DM], xb2[:, u, 0:DM], ALU.add).then_inc(r_s, 1)
                if F:
                    bias(0)
                if T:
                    dve.wait_ge(r_s, j - 1)
                    dve.bn_stats(stats2[:, :], r2[:, u, :]).then_inc(ln2, 1)
                if G:
                    relu_lo(2 * j, 1)
                if T:
                    done = known(dve, 2 * (j - 1) - 1)
                    dve.wait_ge(const_v, 1)
                    dve.wait_ge(ln2, done)
                    dve.bn_aggr(mv2[:, :], stats2[:, :]).then_inc(ln2, 1)
                if F:
                    bias(1)
                if T:
                    dve.wait_ge(std_s, j - 1)
                    dve.reciprocal(rstd2[:, :], std2[:, :]).then_inc(rec, 1)
                if F:
                    x_lo(j + 1, 1 - u)
                if T:
                    dve.wait_ge(rec, j - 1)
                    dve.tensor_scalar(o_t[:, u, :], r2[:, u, :], mv2[:, 0:1], rstd2[:, 0:1],
                                      ALU.subtract, ALU.mult).then_inc(o_s, 1)
                if F:
                    relu_lo(2 * j + 1, 0)

            phase2(dve, slot)

        @block.tensor
        def _(pe):
            def three(dst, terms, sig):
                n = 3 * len(terms)
                i = 0
                for sh, sl, mh, ml in terms:
                    for a, b in ((sh, mh), (sh, ml), (sl, mh)):
                        last = pe.matmul(dst, a, b, start=(i == 0), stop=(i == n - 1))
                        i += 1
                last.then_inc(sig, 1)

            def in_proj(dst, q, c0, sig):
                three(dst, [(win[:, 0, k, c0:c0 + P], win[:, 1, k, c0:c0 + P], xs[:, q, 0, k, :], xs[:, q, 1, k, :])
                            for k in range(KD)], sig)

            pe.wait_ge(const_p, 1)
            pe.wait_ge(const_v, 1)
            pe.wait_ge(in_small, 96)

            def step(g, u, stages):
                it = 2 * g + u
                A, B, C = "A" in stages, "B" in stages, "C" in stages
                if A:
                    pe.wait_ge(xlo, KD * (it + 1))
                    if isinstance(g, int) and g == 0 and u == 0:
                        pe.wait_ge(wlo, 1)
                    for b in range(KI):
                        if late(g) or u or b >= 2:
                            pe.wait_ge(cin_done, KI * it + b - 1)
                        in_proj(bank[CONV0 + b % 2][:, :], u, b * P, conv_mm)
                if C:
                    pe.wait_ge(norm, SUB * (it - 1))
                    pe.wait_ge(sg_done, KI * (it - 1))
                    for k in range(KD):
                        for j in range(SUB):
                            last = pe.transpose(bank[GATE0 + k][:, j * P:(j + 1) * P],
                                                x1row[:, u, j, k * P:(k + 1) * P], ident[:, :])
                        last.then_inc(x1T_mm, 1)
                if B:
                    pe.wait_ge(scan_s, SCAN * it)
                    if late(g):
                        pe.wait_ge(skip, KI * (it - 1))
                    pe.matmul(bank[SSM][:, :], ones16[:, :], dB[:, :], start=True, stop=True).then_inc(ssm_mm, 1)

                def gates(bs):
                    for b in bs:
                        if C and b < 2:
                            pe.wait_ge(x1T_done, KD * (it - 2) + b + 1)
                        if b >= 2:
                            pe.wait_ge(sg_done, KI * (it - 1) + b - 1)
                        if isinstance(g, int) and g == 0 and b == 0:
                            pe.wait_ge(wlo, 2)
                        in_proj(bank[GATE0 + b % 2][:, :], 1 - u, DI + b * P, gate_mm)

                if B:
                    gates((0, 1))
                if C:
                    pe.wait_ge(x1T_done, KD * (it - 1))
                    for j in range(SUB):
                        for k in range(KD):
                            last = pe.matmul(bank[SMALL][:, R0 + j * NE:R0 + (j + 1) * NE], x1T[:, k, j * P:(j + 1) * P],
                                             wr_s[:, k, :], start=(k == 0), stop=(k == KD - 1))
                    last.then_inc(logit_mm, 1)
                if B:
                    gates((2, 3))
                if C:
                    pe.wait_ge(onehot, it - 1)
                    for j in range(SUB + 1):
                        dst = bank[SMALL][:, RK + j * NE:RK + (j + 1) * NE]
                        for i in range(j):
                            last = pe.matmul(dst, ones[:, :], oh[:, i, :], start=(i == 0), stop=(j == SUB and i == j - 1))
                        if j < SUB:
                            pe.matmul(dst, tri[:, :], oh[:, j, :], start=(j == 0), stop=True)
                    last.then_inc(rank_mm, 1)
                if A:
                    pe.wait_ge(cvlo, KI * (it + 1))
                    if isinstance(g, int) and g == 0 and u == 0:
                        pe.wait_ge(wlo, 3)
                    if C:
                        pe.wait_ge(base_set, it)
                    three(bank[SMALL][0:XDBL_M, :],
                          [(wx[:, 0, b, :], wx[:, 1, b, :], cvs[:, 0, b, :], cvs[:, 1, b, :]) for b in range(KI)], xdbl_mm)
                if B:
                    pe.wait_ge(golo, KI * it)
                    if isinstance(g, int) and g == 0:
                        pe.wait_ge(wlo, 4)
                    for j in range(SUB):
                        if late(g) or j >= 2:
                            pe.wait_ge(resd, SUB * (it - 1) + j - 1)
                        three(bank[OUT0 + j % 2][:, 0:DM],
                              [(gos[:, 0, b, j * P:(j + 1) * P], gos[:, 1, b, j * P:(j + 1) * P], wout[:, 0, b, :], wout[:, 1, b, :])
                               for b in range(KI)], out_mm)

            phase1(pe, step)
            pe.wait_ge(tab_ready, 1)

            def x_transpose(g, u, j):
                pe.wait_ge(in_row[u], 16 * (g + 1))
                for k in range(KD):
                    last = pe.transpose(bank[XGT][:, k * P:(k + 1) * P], xrow[:, u, k * P:(k + 1) * P], ident[:, :])
                last.then_inc(xg_mm, 1)

            x_transpose(0, 0, 0)

            def slot(g, u, stages):
                j = 2 * g + u
                F, G = "F" in stages, "G" in stages
                if F:
                    e = pe.value_load(tab[0:1, T_E, bass.ds(j, 1)], min_val=0, max_val=NE - 1)
                    v = pe.value_load(tab[0:1, T_BUF, bass.ds(j, 1)], min_val=0, max_val=1)
                if G:
                    vp = pe.value_load(tab[0:1, T_BUF, bass.ds(j - 1, 1)], min_val=0, max_val=1)

                def up(half_no):
                    c0 = half_no * 512
                    three(bank[HID0 + half_no][:, :],
                          [(xg[:, u, 0, k, :], xg[:, u, 1, k, :],
                            wsp[:, v, k * FF + c0:k * FF + c0 + 512],
                            wsp[:, v, W1N + k * FF + c0:W1N + k * FF + c0 + 512]) for k in range(KD)], hid_mm)

                def turn(half_no):
                    for b in range(4):
                        last = pe.transpose(bank[HIDT0 + half_no][:, b * P:(b + 1) * P], h[:, half_no, b * P:(b + 1) * P], ident[:, :])
                    last.then_inc(hT_mm, 1)

                def down(half_no):
                    dst = bank[Y0 + 1 - u][:, 0:DM]
                    for b in range(4 * half_no, 4 * half_no + 4):
                        wh = wsp[:, vp, WHALF + b * DM:WHALF + (b + 1) * DM]
                        wl = wsp[:, vp, WHALF + W1N + b * DM:WHALF + W1N + (b + 1) * DM]
                        pe.matmul(dst, hT[:, 0, b, :], wh, start=(b == 0), stop=False)
                        pe.matmul(dst, hT[:, 0, b, :], wl, start=False, stop=False)
                        last = pe.matmul(dst, hT[:, 1, b, :], wh, start=False, stop=(b == KF - 1))
                    if half_no:
                        last.then_inc(y_mm, 1)

                if F:
                    pe.wait_ge(ehi, PIECES * (e + 1))
                    pe.wait_ge(elo, PIECES * (e + 1))
                    if late(g) or u:
                        pe.wait_ge(evac, 2 * j - 1)
                    pe.wait_ge(xglo, j + 1)
                    up(0)
                if G:
                    pe.wait_ge(evac, 2 * j)
                    if late(g):
                        pe.wait_ge(hTlo, 2 * j - 2)
                    turn(1)
                    pe.wait_ge(hTlo, 2 * j - 1)
                    if not isinstance(g, int) or j > 2:
                        pe.wait_ge(r_s, j - 2)
                    down(0)
                if F:
                    if late(g) or u:
                        pe.wait_ge(evac, 2 * j)
                    up(1)
                    pe.wait_ge(xglo, j + 1)
                    x_transpose(g + u, 1 - u, j + 1)
                    pe.wait_ge(evac, 2 * j + 1)
                    turn(0)
                if G:
                    pe.wait_ge(hTlo, 2 * j)
                    down(1)

            phase2(pe, slot)


_INS = ["xT", "x", "w_in", "conv_w", "conv_b", "w_x", "a_log", "d_par", "w_out", "wr", "br", "w1", "b1", "w2", "b2"]


def kernel(L0_attn_input_tensor, L0_attn_W_in, L0_attn_conv_w, L0_attn_conv_b, L0_attn_W_x, L0_attn_A_log,
           L0_attn_D_param, L0_attn_W_out, L0_ffn_Wr, L0_ffn_br, L0_ffn_W1, L0_ffn_b1, L0_ffn_W2, L0_ffn_b2):
    import numpy as np
    import concourse.bacc as bacc
    from concourse.bass_utils import run_bass_kernel_spmd

    x = np.asarray(L0_attn_input_tensor).reshape(TOKENS, DM)
    w_x = np.asarray(L0_attn_W_x)
    cols = [0] * XDBL_M
    for n in range(NST):
        cols[B_ROW + n] = 1 + n
        cols[C_ROW + n] = 1 + NST + n
    arrays = {
        "xT": x.T, "x": x, "w_in": L0_attn_W_in, "conv_w": np.asarray(L0_attn_conv_w).reshape(DI, TAPS),
        "conv_b": np.asarray(L0_attn_conv_b).reshape(KI, P).T, "w_x": w_x[:, cols], "a_log": L0_attn_A_log, "d_par": np.asarray(L0_attn_D_param).reshape(KI, P).T,
        "w_out": L0_attn_W_out, "wr": np.asarray(L0_ffn_Wr).T, "br": L0_ffn_br,
        "w1": np.asarray(L0_ffn_W1).transpose(0, 2, 1), "b1": L0_ffn_b1,
        "w2": np.asarray(L0_ffn_W2).transpose(0, 2, 1), "b2": L0_ffn_b2,
    }
    arrays = {k: np.ascontiguousarray(v) for k, v in arrays.items()}
    nc = bacc.Bacc("TRN2", target_bir_lowering=False, num_devices=1)
    args = [nc.dram_tensor(n, arrays[n].shape, F32, kind="ExternalInput").ap() for n in _INS]
    out = nc.dram_tensor("out", (TOKENS, DM), F32, kind="ExternalOutput").ap()
    build(nc, *args, out)
    r = run_bass_kernel_spmd(nc, [arrays], core_ids=[0])
    return np.asarray(r.results[0]["out"]).reshape(1, TOKENS, DM)
```
